# Optimizing a Trainium2 kernel written in Bass

```python
import numpy as np
import jax
import jax.numpy as jnp

def _softmax(x, axis=-1):
    return jax.nn.softmax(x, axis=axis)

def _gelu(x):
    return jax.nn.gelu(x, approximate=True)

def _silu(x):
    return jax.nn.silu(x)

def _sigmoid(x):
    return jax.nn.sigmoid(x)

def _layernorm(x, axis=-1, eps=1e-05):
    m = jnp.mean(x, axis=axis, keepdims=True)
    v = jnp.var(x, axis=axis, keepdims=True)
    return (x - m) / jnp.sqrt(v + eps)

def _scatter_add(tgt, idx, src, axis=0):
    return tgt.at[idx].add(src)

def _segment_sum(src, seg, n):
    return jax.ops.segment_sum(src, seg, n)
kernel_name = 'mk_xattn_seq_d1_seqx_r4_d89dcf'

def setup_inputs(seed: int=0):
    np.random.seed(seed)
    _w = jnp.asarray

    def _rec_inputs():
        import jax
        import jax.numpy as jnp
        _rk = jax.random.key(seed)
        x = -0.000125 + 0.9999 * jax.random.normal(jax.random.fold_in(_rk, 1), (8, 256, 1024), jnp.float32)
        _lenS = 256 - jax.random.randint(jax.random.fold_in(_rk, 7), (8,), 0, max(1, 256 // 4) + 1, jnp.int32)
        _lenS2 = 256 - jax.random.randint(jax.random.fold_in(_rk, 8), (8,), 0, max(1, 256 // 4) + 1, jnp.int32)
        _ctx_4096P = jax.random.normal(jax.random.fold_in(_rk, 11), (8, 16, 1024), jnp.float32)
        _ctx_4096c = jax.random.dirichlet(jax.random.fold_in(_rk, 511), 0.3 * jnp.ones((16,), jnp.float32), (8, 256))
        _ctx_4096t = jnp.einsum('bsk,bkd->bsd', _ctx_4096c, _ctx_4096P)
        _ctx_4096t = _ctx_4096t * jax.lax.rsqrt(jnp.mean(jnp.square(_ctx_4096t)) + 1e-12) * 0.953939
        ctx_4096 = 0.000227908 + 0.99994 * (_ctx_4096t + 0.3 * jax.random.normal(jax.random.fold_in(_rk, 611), (8, 256, 1024), jnp.float32))
        _validS = jnp.arange(256)[None, :] < _lenS[:, None]
        _validS2 = jnp.arange(256)[None, :] < _lenS2[:, None]
        _causal = jnp.tril(jnp.ones((256, 256), dtype=bool))
        mask_BxS2_bf1 = jnp.ones((8, 256), dtype=bool)
        return (x, ctx_4096, mask_BxS2_bf1)
    x, ctx_4096, mask_BxS2_bf1 = _rec_inputs()

    def _L0_xattn_setup():
        import jax, jax.numpy as jnp
        import numpy as np
        HIDDEN = 1024
        HEADS = 32
        HEAD_DIM = HIDDEN // HEADS
        LN_EPS = 1e-05

        def _split_heads(x):
            B, S, _ = x.shape
            return x.reshape(B, S, HEADS, HEAD_DIM).transpose(0, 2, 1, 3)
        key = jax.random.key(seed)
        ks = jax.random.split(key, 7)
        B, S, SLOTS = (2, 1024, 128)
        hidden_states = jax.random.normal(ks[0], (B, S, HIDDEN), dtype=jnp.float32)
        memory_keys = jax.random.normal(ks[1], (B, SLOTS, HIDDEN), dtype=jnp.float32)
        memory_values = jax.random.normal(ks[2], (B, SLOTS, HIDDEN), dtype=jnp.float32)
        attention_mask = jnp.ones((B, SLOTS), dtype=jnp.bool_)
        Wq = jax.random.normal(ks[3], (HIDDEN, HIDDEN), dtype=jnp.float32) / np.sqrt(HIDDEN)
        Wout = jax.random.normal(ks[4], (HIDDEN, HIDDEN), dtype=jnp.float32) / np.sqrt(HIDDEN)
        ln_gamma = jnp.ones((HIDDEN,), dtype=jnp.float32)
        ln_beta = jnp.zeros((HIDDEN,), dtype=jnp.float32)
        return dict(hidden_states=hidden_states, memory_keys=memory_keys, memory_values=memory_values, attention_mask=attention_mask, Wq=Wq, Wout=Wout, ln_gamma=ln_gamma, ln_beta=ln_beta)
    _L0_xattn_all = _L0_xattn_setup()
    _L0_xattn_in = {k: v for k, v in _L0_xattn_all.items() if k in ('Wq', 'Wout', 'ln_gamma', 'ln_beta')}
    del _L0_xattn_all
    return {'x': x, 'ctx_4096': ctx_4096, 'mask_BxS2_bf1': mask_BxS2_bf1, 'L0_xattn_Wq': _L0_xattn_in['Wq'], 'L0_xattn_Wout': _L0_xattn_in['Wout'], 'L0_xattn_ln_gamma': _L0_xattn_in['ln_gamma'], 'L0_xattn_ln_beta': _L0_xattn_in['ln_beta']}

def reference(x, ctx_4096, mask_BxS2_bf1, L0_xattn_Wq, L0_xattn_Wout, L0_xattn_ln_gamma, L0_xattn_ln_beta):
    import jax
    import jax.numpy as jnp

    def _L0_xattn_ref(hidden_states, memory_keys, memory_values, attention_mask, Wq, Wout, ln_gamma, ln_beta):
        import jax, jax.numpy as jnp
        import numpy as np
        HIDDEN = 1024
        HEADS = 32
        HEAD_DIM = HIDDEN // HEADS
        LN_EPS = 1e-05

        def _split_heads(x):
            B, S, _ = x.shape
            return x.reshape(B, S, HEADS, HEAD_DIM).transpose(0, 2, 1, 3)
        residual = hidden_states
        mu = jnp.mean(hidden_states, axis=-1, keepdims=True)
        var = jnp.var(hidden_states, axis=-1, keepdims=True)
        x = (hidden_states - mu) * jax.lax.rsqrt(var + LN_EPS) * ln_gamma + ln_beta
        Q = _split_heads(x @ Wq.T)
        K = _split_heads(memory_keys)
        V = _split_heads(memory_values)
        scale = HEAD_DIM ** (-0.5)
        scores = jnp.einsum('bhsd,bhtd->bhst', Q, K) * scale
        mask = attention_mask[:, None, None, :]
        scores = jnp.where(mask, scores, -jnp.inf)
        probs = jax.nn.softmax(scores, axis=-1)
        attn = jnp.einsum('bhst,bhtd->bhsd', probs, V)
        B, _, S, _ = attn.shape
        attn = attn.transpose(0, 2, 1, 3).reshape(B, S, HIDDEN)
        out = attn @ Wout.T
        return residual + out
    x = _L0_xattn_ref(x, ctx_4096, ctx_4096, mask_BxS2_bf1, L0_xattn_Wq, L0_xattn_Wout, L0_xattn_ln_gamma, L0_xattn_ln_beta)
    return x

_drawn_inputs = setup_inputs


def setup_inputs(seed=0):
    import zlib

    import numpy as np

    out = dict(_drawn_inputs(seed))
    spreads = {'L0_xattn_ln_gamma': (1.0, 0.2), 'L0_xattn_ln_beta': (0.0, 0.362)}
    factors = {}
    for name, (base, spread) in spreads.items():
        noise = np.random.default_rng([zlib.crc32(name.encode()), seed]).standard_normal(out[name].shape)
        drawn = base * np.exp(spread * noise) if base else spread * noise
        out[name] = jnp.asarray(drawn.astype(out[name].dtype))
    for name, factor in factors.items():
        out[name] = (out[name] * factor).astype(out[name].dtype)
    return out
```

```python
from contextlib import ExitStack

import numpy as np

import concourse.bass as bass
from concourse import mybir
from concourse.alu_op_type import AluOpType as ALU

F32 = mybir.dt.float32
F16 = mybir.dt.float16
U8 = mybir.dt.uint8
I32 = mybir.dt.int32
ACT = mybir.ActivationFunctionType
AX = mybir.AxisListType

B, S, D = 8, 256, 1024
H = 32
DH = D // H
P = 128
KT = D // P
ST = S // P
J = P // DH
G = H // J
LN_EPS = 1e-5
SCALE = float(DH) ** -0.5
W_SCALE = 8.0
M_UNIT = 64.0
PASSES = ((0, 0), (0, 1), (1, 0))
FILLS = 4
STEPS = G * ST
DMA = 16
STACK_DMAS = 3 * J + 1
HALF = G // 2
NEWTON = 3
RSTD_STEPS = 3 + 4 * NEWTON


def xattn(nc, x, ctx_in, mask, wq, wout, gamma, beta, out):
    es = ExitStack()
    with es:
        def sb(name, shape, dt):
            return es.enter_context(nc.sbuf_tensor(name, shape, dt))

        def sem(name):
            return es.enter_context(nc.semaphore(name))

        wqT = sb("wqT", [P, 2, KT, D], F16)
        woT = sb("woT", [P, 2, KT, D], F16)
        q_stack = sb("q_stack", [P, 2, J, G // 2, S], F16)
        k_stack = sb("k_stack", [P, 2, J, G // 2, S], F16)
        zT = sb("zT", [P, 2, KT, S], F16)
        qT = sb("qT", [P, 2, G, S], F16)
        kT = sb("kT", [P, 2, G, S], F16)
        aT = sb("aT", [P, 2, G, S], F16)
        probs = sb("probs", [P, 2, ST, J, S], F32)
        psum_t = sb("probs_sum", [P, J, S], F32)
        v_nat = sb("v_nat", [P, ST, D], F32)
        c_nat = sb("c_nat", [P, ST, D], F32)
        x_nat = sb("x_nat", [P, ST, D], F32)
        den = sb("den", [P, S], F32)
        att = sb("att", [P, 2, S], F32)
        res = sb("res", [P, 2, 512], F32)
        o_buf = sb("o_buf", [P, 2, 512], F32)
        gamma_b = sb("gamma_b", [P, D], F32)
        beta_b = sb("beta_b", [P, D], F32)
        q_bias = sb("q_bias", [P, KT], F32)
        ident = sb("ident", [P, P], F32)
        ones_v = sb("ones_v", [P, DH], F32)
        maxes = sb("maxes", [P, ST, 2, J, G // 2], F32)
        m_rows = sb("m_rows", [H, S], F16)
        rows = sb("rows", [1, 2, S], F16)
        mask_u8 = sb("mask_u8", [1, B, S], U8)
        mask_add = sb("mask_add", [1, B, S], F16)
        stats = sb("stats", [P, ST, 2, 6], F32)
        mean_var = sb("mean_var", [P, ST, 2], F32)
        rstd = sb("rstd", [P, ST], F32)
        var_eps = sb("var_eps", [P, ST], F32)
        newton = sb("newton", [P, ST], F32)
        w_nat = probs[:].rearrange("p a t j s -> p (a t) (j s)")

        score = [es.enter_context(nc.psum_tensor(f"score{i}", [P, J, S], F32)) for i in range(2)]
        pv = [es.enter_context(nc.psum_tensor(f"pv{i}", [P, 2, S], F32)) for i in range(2)]
        mm = [es.enter_context(nc.psum_tensor(f"mm{i}", [P, 512], F32)) for i in range(2)]

        gb_in, mask_in = sem("gb_in"), sem("mask_in")
        w_in = [sem(f"w_in{i}") for i in range(4)]
        x_in, c_in, v_in = sem("x_in"), sem("c_in"), sem("v_in")
        res_in = [sem(f"res_in{i}") for i in range(2)]
        out_done = [sem(f"out_done{i}") for i in range(2)]
        row_in, k_in, q_in = sem("row_in"), [sem(f"k_in{i}") for i in range(2)], [sem(f"q_in{i}") for i in range(2)]
        m_in = sem("m_in")
        consts, ident0, ident_ok, gamma_ok, stack0 = sem("consts"), sem("ident0"), sem("ident_ok"), sem("gamma_ok"), sem("stack0")
        mask_f, mask_ok = sem("mask_f"), sem("mask_ok")
        bias_done, wg_done, wq_ready, wq_hi, wq_lo = sem("bias_done"), sem("wg_done"), sem("wq_ready"), sem("wq_hi"), sem("wq_lo")
        wo_ready, wo_hi, wo_lo = sem("wo_ready"), sem("wo_hi"), sem("wo_lo")
        bn_done, aggr_done, rstd_step, z_done = sem("bn_done"), sem("aggr_done"), sem("rstd_step"), sem("z_done")
        kt_ready, k_hi, k_lo = sem("kt_ready"), sem("k_hi"), sem("k_lo")
        zt_ready, z_hi, z_lo = sem("zt_ready"), sem("z_hi"), sem("z_lo")
        q_ready, q_hi, q_lo = sem("q_ready"), sem("q_hi"), sem("q_lo")
        s_ready, max_done, mt_ready, m_done = sem("s_ready"), sem("max_done"), sem("mt_ready"), sem("m_done")
        t_ready, exp_done, padd_done, pv_ready = sem("t_ready"), sem("exp_done"), sem("padd_done"), sem("pv_ready")
        den_done, att_done, a_hi, a_lo = sem("den_done"), sem("att_done"), sem("a_hi"), sem("a_lo")
        o_ready, o_done = sem("o_ready"), sem("o_done")

        WO_FILLS = 2 * KT
        block = es.enter_context(nc.Block())

        K_STEPS, Z_STEPS = (1, 2, 9, 10), (3, 4, 5, 6)

        Q_SPLITS = (1, 4, 6)

        @block.sync
        def _(sp):
            def load_x(a):
                sp.dma_start(x_nat[:], x[a].rearrange("(c p) d -> p c d", p=P)).then_inc(x_in, DMA)

            def load_c(a):
                sp.dma_start(c_nat[:], ctx_in[a].rearrange("(c p) d -> p c d", p=P)).then_inc(c_in, DMA)

            def load_w(n):
                if n >= KT + 4:
                    sp.wait_ge(wo_ready, 2 * (n - KT - 4) + 2)
                elif n >= 4:
                    sp.wait_ge(wq_ready, n - 3)
                w = wq if n < KT else wout
                m = n % KT
                sp.dma_start(w_nat[:, n % 4], w[m * P:(m + 1) * P, :]).then_inc(w_in[n % 4], DMA)

            def fill_k_stack(a, h, t_count):
                if t_count is not None:
                    sp.wait_ge(t_ready, t_count)
                for j in range(J):
                    for r, part in enumerate((0, 0, 1)):
                        sp.dma_start(k_stack[DH * r:DH * (r + 1), h, j],
                                     kT[DH * j:DH * (j + 1), part, h * HALF:(h + 1) * HALF, :]).then_inc(k_in[h], DMA)
                sp.dma_start(k_stack[96:97, h].rearrange("o j g s -> o (j g) s"),
                             mask_add[0:1, a, :].unsqueeze(1).to_broadcast([1, J * HALF, S])).then_inc(k_in[h], DMA)

            def fill_q_stack(a, h):
                sp.wait_ge(q_lo, a * FILLS + 2 * h + 2)
                for j in range(J):
                    for r, part in enumerate((0, 1, 0)):
                        sp.dma_start(q_stack[DH * r:DH * (r + 1), h, j],
                                     qT[DH * j:DH * (j + 1), part, h * HALF:(h + 1) * HALF, :]).then_inc(q_in[h], DMA)
                sp.dma_start(q_stack[97:98, h], q_stack[98:99, h]).then_inc(q_in[h], DMA)

            def load_res(c, i):
                if i >= 2:
                    sp.wait_ge(o_done, c * FILLS + i - 1)
                st, nh = i // 2, i % 2
                sp.dma_start(res[:, i % 2, :], x[c, st * P:(st + 1) * P, nh * 512:(nh + 1) * 512]).then_inc(res_in[i % 2], DMA)

            def store_out(c, i):
                sp.wait_ge(o_done, c * FILLS + i + 1)
                st, nh = i // 2, i % 2
                sp.dma_start(out[c, st * P:(st + 1) * P, nh * 512:(nh + 1) * 512], o_buf[:, i % 2, :]).then_inc(out_done[i % 2], DMA)

            def iteration(b, first, last, more):
                if not first:
                    sp.wait_ge(pv_ready, b * G)
                sp.dma_start(v_nat[:], ctx_in[b].rearrange("(c p) d -> p c d", p=P)).then_inc(v_in, DMA)
                if not first:
                    load_res(b - 1, 0)
                    load_res(b - 1, 1)
                    store_out(b - 1, 0)
                    load_res(b - 1, 2)
                    store_out(b - 1, 1)
                    load_res(b - 1, 3)
                if not first and not last:
                    store_out(b - 1, 2)
                sp.wait_ge(m_done, b + 1)
                sp.dma_start(q_stack[97:98].rearrange("o h j g s -> o (h j g) s"), m_rows[:]).then_inc(m_in, DMA)
                if last:
                    store_out(b - 1, 2)
                if not first:
                    store_out(b - 1, 3)
                if more:
                    sp.wait_ge(zt_ready, (b + 2) * FILLS)
                    load_x(b + 2)
                if not last:
                    sp.wait_ge(k_lo, (b + 2) * FILLS)
                if more:
                    load_c(b + 2)
                if not last:
                    fill_k_stack(b + 1, 0, b * STEPS + STEPS // 2)
                    fill_q_stack(b + 1, 0)
                    fill_k_stack(b + 1, 1, b * STEPS + STEPS)
                    fill_q_stack(b + 1, 1)

            load_w(0)
            sp.dma_start(beta_b[:], beta.rearrange("(a d) -> a d", a=1).to_broadcast([P, D])).then_inc(gb_in, DMA)
            sp.dma_start(gamma_b[:], gamma.rearrange("(a d) -> a d", a=1).to_broadcast([P, D])).then_inc(gb_in, DMA)
            load_w(1)
            load_x(0)
            load_w(2)
            load_w(3)
            sp.dma_start(mask_u8[:], mask.rearrange("(o b) s -> o b s", o=1)).then_inc(mask_in, DMA)
            load_c(0)
            for n in range(4, KT):
                load_w(n)
            sp.wait_ge(z_lo, FILLS)
            load_x(1)
            sp.wait_ge(k_lo, FILLS)
            load_c(1)
            sp.wait_ge(consts, 3)
            sp.wait_ge(stack0, 2)
            sp.dma_start(q_stack[96:97].rearrange("o h j g s -> o (h j g) s"), rows[0:1, 0, :].unsqueeze(1).to_broadcast([1, H, S])).then_inc(row_in, DMA)
            sp.dma_start(k_stack[97:98].rearrange("o h j g s -> o (h j g) s"), rows[0:1, 1, :].unsqueeze(1).to_broadcast([1, H, S])).then_inc(row_in, DMA)
            sp.wait_ge(mask_ok, 1)
            fill_k_stack(0, 0, None)
            fill_q_stack(0, 0)
            fill_k_stack(0, 1, None)
            fill_q_stack(0, 1)
            for n in range(KT, 2 * KT):
                load_w(n)
            iteration(0, True, False, True)
            with sp.Fori(1, B - 2) as b:
                iteration(b, False, False, True)
            iteration(B - 2, False, False, False)
            iteration(B - 1, False, True, False)
            load_res(B - 1, 0)
            load_res(B - 1, 1)
            store_out(B - 1, 0)
            load_res(B - 1, 2)
            store_out(B - 1, 1)
            load_res(B - 1, 3)
            store_out(B - 1, 2)
            store_out(B - 1, 3)
            for i in range(2):
                sp.wait_ge(out_done[i], B * 2 * DMA)

        @block.gpsimd
        def _(pool):
            pool.memset(ident[:], 0.0).then_inc(ident0, 1)
            pool.wait_ge(ident0, 1)
            pool.affine_select(out=ident[:], in_=ident[:], compare_op=ALU.not_equal, fill=1.0, base=0,
                               pattern=[[-1, P]], channel_multiplier=1).then_inc(ident_ok, 1)
            pool.wait_ge(gb_in, 2 * DMA)
            for m in range(KT):
                pool.wait_ge(bias_done, m + 1)
                pool.tensor_tensor(w_nat[:, m % 4], w_nat[:, m % 4], gamma_b[:], ALU.mult).then_inc(wg_done, 1)
            pool.wait_ge(wg_done, KT)
            for n, stack in enumerate((q_stack, k_stack)):
                if n:
                    pool.wait_ge(stack0, n)
                pool.memset(stack[96:128].rearrange("p h j g s -> p (h j g s)").bitcast(F32), 0.0).then_inc(stack0, 1)

            def iteration(b, first):
                for g in range(G):
                    pool.wait_ge(exp_done, b * STEPS + 2 * g + 2)
                    if not (first and g == 0):
                        pool.wait_ge(pv_ready, b * G + g)
                    pool.tensor_tensor(psum_t[:], probs[:, g % 2, 0], probs[:, g % 2, 1], ALU.add).then_inc(padd_done, 1)

            iteration(0, True)
            with pool.Fori(1, B) as b:
                iteration(b, False)

        @block.tensor
        def _(pe):
            def wq_transposes(m):
                pe.wait_ge(w_in[m % 4], (m // 4 + 1) * DMA)
                pe.wait_ge(wg_done, m + 1)
                if m >= 2:
                    pe.wait_ge(wq_lo, m - 1)
                flat = score[m % 2][:].rearrange("p j s -> p (j s)")
                for k in range(KT):
                    last = pe.transpose(flat[:, k * P:(k + 1) * P], w_nat[:, m % 4, k * P:(k + 1) * P], ident[:])
                last.then_inc(wq_ready, 1)

            def wo_transposes(f):
                m, h = f // 2, f % 2
                pe.wait_ge(w_in[m % 4], ((KT + m) // 4 + 1) * DMA)
                if f < 2:
                    pe.wait_ge(q_lo, 3 + f)
                else:
                    pe.wait_ge(wo_lo, f - 1)
                for n in range(4):
                    k = 4 * h + n
                    last = pe.transpose(mm[f % 2][:, n * P:(n + 1) * P], w_nat[:, m % 4, k * P:(k + 1) * P], ident[:])
                last.then_inc(wo_ready, 1)

            def k_transposes(a, i, b):
                if i == 0:
                    pe.wait_ge(c_in, (a + 1) * DMA)
                if i >= 2:
                    pe.wait_ge(z_lo, a * FILLS + i + 1)
                elif b is not None:
                    pe.wait_ge(att_done, b * G)
                for n in range(4):
                    g, tt = 2 * i + n // 2, n % 2
                    last = pe.transpose(pv[i % 2][:, n // 2, tt * P:(tt + 1) * P], c_nat[:, tt, g * P:(g + 1) * P], ident[:])
                last.then_inc(kt_ready, 1)

            def z_transposes(a, i):
                if i == 0:
                    pe.wait_ge(z_done, (a + 1) * ST)
                if i < 2:
                    pe.wait_ge(k_lo, a * FILLS + i + 1)
                else:
                    pe.wait_ge(z_lo, a * FILLS + i - 1)
                for n in range(4):
                    k, st = 2 * i + n // 2, n % 2
                    last = pe.transpose(pv[i % 2][:, n // 2, st * P:(st + 1) * P], x_nat[:, st, k * P:(k + 1) * P], ident[:])
                last.then_inc(zt_ready, 1)

            Q_MM = 2 * KT * 3

            def q_matmuls(a, lo, hi, c):
                for u in range(lo, hi):
                    i, v = divmod(u, Q_MM)
                    m2, v2 = divmod(v, KT * 3)
                    k, p = divmod(v2, 3)
                    if u == 0:
                        pe.wait_ge(z_lo, (a + 1) * FILLS)
                    if v == 0 and i >= 2:
                        pe.wait_ge(q_lo, a * FILLS + i - 1)
                    elif v == 0 and c is not None:
                        pe.wait_ge(o_done, c * FILLS + i + 3)
                    elif v == 0 and not (isinstance(a, int) and a == 0):
                        pe.wait_ge(wo_lo, WO_FILLS - 1 + i)
                    m = 2 * i + m2
                    wp, zp = PASSES[p]
                    last = pe.matmul(mm[i % 2][:, m2 * S:(m2 + 1) * S], wqT[:, wp, k, m * P:(m + 1) * P], zT[:, zp, k, :],
                                     start=(v2 == 0), stop=(v2 == KT * 3 - 1))
                    if v == Q_MM - 1:
                        last.then_inc(q_ready, 1)

            O_MM = KT * 3

            def o_matmuls(c, lo, hi, q_before):
                for u in range(lo, hi):
                    i, v = divmod(u, O_MM)
                    k, p = divmod(v, 3)
                    st, nh = i // 2, i % 2
                    if u == 0:
                        pe.wait_ge(a_lo, c * G + G - 1)
                    if u == (KT - 1) * 3:
                        pe.wait_ge(a_lo, (c + 1) * G)
                    if v == 0 and i >= 2:
                        pe.wait_ge(o_done, c * FILLS + i - 1)
                    elif v == 0 and q_before:
                        pe.wait_ge(q_lo, (c + 1) * FILLS + i + 3)
                    elif v == 0:
                        pe.wait_ge(o_done, (c - 1) * FILLS + i + 3)
                    ap, wp = PASSES[p]
                    last = pe.matmul(mm[i % 2][:], aT[:, ap, k, st * P:(st + 1) * P], woT[:, wp, k, nh * 512:(nh + 1) * 512],
                                     start=(v == 0), stop=(v == O_MM - 1))
                    if v == O_MM - 1:
                        last.then_inc(o_ready, 1)

            def scores_s(b, n, first):
                g, st = n // 2, n % 2
                h, gl = divmod(g, HALF)
                if n in (0, STEPS // 2):
                    pe.wait_ge(k_in[g // HALF], (b + 1) * STACK_DMAS * DMA)
                    pe.wait_ge(q_in[g // HALF], (b + 1) * STACK_DMAS * DMA)
                if n >= 2:
                    pe.wait_ge(max_done, b * STEPS + n - 1)
                elif not first:
                    pe.wait_ge(exp_done, b * STEPS + n - 1)
                else:
                    pe.wait_ge(wq_lo, KT - 1 + n)
                for j in range(J):
                    last = pe.matmul(score[n % 2][:, j, :], q_stack[:, h, j, gl, st * P:(st + 1) * P], k_stack[:, h, j, gl, :],
                                     start=True, stop=True)
                last.then_inc(s_ready, 1)

            def max_transposes(b, last_batch):
                pe.wait_ge(max_done, (b + 1) * STEPS)
                if last_batch:
                    pe.wait_ge(att_done, b * G)
                else:
                    pe.wait_ge(k_lo, (b + 1) * FILLS + 3)
                for st in range(ST):
                    last = pe.transpose(pv[0][0:H, 0, st * P:(st + 1) * P], maxes[:, st].rearrange("p h j g -> p (h j g)"), ident[:])
                last.then_inc(mt_ready, 1)

            def scores_t(b, n):
                g, tt = n // 2, n % 2
                h, gl = divmod(g, HALF)
                if n == 0:
                    pe.wait_ge(m_in, (b + 1) * DMA)
                if n < 2:
                    pe.wait_ge(max_done, b * STEPS + STEPS - 1 + n)
                else:
                    pe.wait_ge(exp_done, b * STEPS + n - 1)
                for j in range(J):
                    last = pe.matmul(score[n % 2][:, j, :], k_stack[:, h, j, gl, tt * P:(tt + 1) * P], q_stack[:, h, j, gl, :],
                                     start=True, stop=True)
                last.then_inc(t_ready, 1)

            def probs_times_v(b, g, last_batch):
                pe.wait_ge(exp_done, b * STEPS + 2 * g + 2)
                if g == 0:
                    pe.wait_ge(v_in, (b + 1) * DMA)
                    pe.wait_ge(m_done, b + 1)
                elif g == 1 and not last_batch:
                    pe.wait_ge(k_lo, (b + 2) * FILLS)
                elif g == 1:
                    pe.wait_ge(att_done, b * G)
                else:
                    pe.wait_ge(att_done, b * G + g - 1)
                for tt in range(ST):
                    for j in range(J):
                        pe.matmul(pv[g % 2][DH * j:DH * (j + 1), 0, :], v_nat[:, tt, g * P + DH * j:g * P + DH * (j + 1)],
                                  probs[:, g % 2, tt, j, :], start=(tt == 0), stop=(tt == ST - 1), skip_group_check=True)
                pe.wait_ge(padd_done, b * G + g + 1)
                for j in range(J):
                    last = pe.matmul(pv[g % 2][DH * j:DH * (j + 1), 1, :], ones_v[:], psum_t[:, j, :],
                                     start=False, stop=True, skip_group_check=True)
                last.then_inc(pv_ready, 1)

            O_AT = [0, 0] + [3 * O_MM * n // 7 for n in range(1, 8)] + [3 * O_MM + 3 * n for n in range(1, 9)]
            O_AT_LAST = [4 * n for n in range(STEPS + 1)] + [80, 88] + [4 * O_MM] * (G - 1)
            Q_AT = [40 + 18 * g for g in range(G)] + [4 * Q_MM]

            def iteration(b, first, last):
                for n in range(STEPS):
                    scores_s(b, n, first)
                    if not last:
                        if n in K_STEPS:
                            k_transposes(b + 1, K_STEPS.index(n), None if first else b)
                        if n in Z_STEPS:
                            z_transposes(b + 1, Z_STEPS.index(n))
                    if first:
                        wo_transposes(n)
                    else:
                        at = O_AT_LAST if last else O_AT
                        o_matmuls(b - 1, at[n], at[n + 1], True)
                max_transposes(b, last)
                if last:
                    o_matmuls(b - 1, O_AT_LAST[STEPS], O_AT_LAST[STEPS + 1], True)
                else:
                    q_matmuls(b + 1, 0, Q_AT[0], None if first else b - 1)
                for g in range(G):
                    scores_t(b, 2 * g)
                    scores_t(b, 2 * g + 1)
                    if last:
                        o_matmuls(b - 1, O_AT_LAST[STEPS + 1 + g], O_AT_LAST[STEPS + 2 + g], True)
                    elif g < G - 1:
                        q_matmuls(b + 1, Q_AT[g], Q_AT[g + 1], None if first else b - 1)
                    if g >= 1:
                        probs_times_v(b, g - 1, last)
                if not last:
                    q_matmuls(b + 1, Q_AT[G - 1], Q_AT[G], None if first else b - 1)
                probs_times_v(b, G - 1, last)

            pe.wait_ge(ident_ok, 1)
            for m in range(KT):
                wq_transposes(m)
            for i in (0, 1):
                k_transposes(0, i, None)
            for i in range(FILLS):
                z_transposes(0, i)
            for i in (2, 3):
                k_transposes(0, i, None)
            pe.wait_ge(wq_lo, KT)
            q_matmuls(0, 0, 4 * Q_MM, None)
            pe.wait_ge(row_in, 2 * DMA)
            pe.wait_ge(consts, 3)
            iteration(0, True, False)
            with pe.Fori(1, B - 1) as b:
                iteration(b, False, False)
            iteration(B - 1, False, True)
            o_matmuls(B - 1, 0, 4 * O_MM, False)

        @block.scalar
        def _(act):
            def wq_split(m):
                act.wait_ge(wq_ready, m + 1)
                act.activation(wqT[:, 0, :, m * P:(m + 1) * P], score[m % 2][:].rearrange("p j (a o) -> p (j a) o", o=P),
                               ACT.Copy, scale=W_SCALE).then_inc(wq_hi, 1)

            def wo_split(f):
                m, h = f // 2, f % 2
                act.wait_ge(wo_ready, f + 1)
                act.activation(woT[:, 0, 4 * h:4 * h + 4, m * P:(m + 1) * P], mm[f % 2][:].rearrange("p (a o) -> p a o", o=P),
                               ACT.Copy, scale=W_SCALE).then_inc(wo_hi, 1)

            def k_split(a, i):
                act.wait_ge(kt_ready, a * FILLS + i + 1)
                if i % 2 == 0 and not (isinstance(a, int) and a == 0):
                    act.wait_ge(k_in[i // 2], a * STACK_DMAS * DMA)
                act.activation(kT[:, 0, 2 * i:2 * i + 2, :], pv[i % 2][:], ACT.Copy).then_inc(k_hi, 1)

            def z_split(a, i):
                act.wait_ge(zt_ready, a * FILLS + i + 1)
                if i == 0 and not (isinstance(a, int) and a == 0):
                    act.wait_ge(q_ready, a * FILLS)
                act.activation(zT[:, 0, 2 * i:2 * i + 2, :], pv[i % 2][:], ACT.Copy).then_inc(z_hi, 1)

            def q_split(a, i):
                act.wait_ge(q_ready, a * FILLS + i + 1)
                if i % 2 == 0 and not (isinstance(a, int) and a == 0):
                    act.wait_ge(q_in[i // 2], a * STACK_DMAS * DMA)
                for m2 in range(2):
                    m = 2 * i + m2
                    last = act.activation(qT[:, 0, m, :], mm[i % 2][:, m2 * S:(m2 + 1) * S], ACT.Identity, bias=q_bias[:, m:m + 1])
                last.then_inc(q_hi, 1)

            def exp_step(b, n, first):
                g, tt = n // 2, n % 2
                act.wait_ge(t_ready, b * STEPS + n + 1)
                if tt == 0 and not (first and g < 2):
                    act.wait_ge(pv_ready, b * G + g - 1)
                act.activation(probs[:, g % 2, tt], score[n % 2][:], ACT.Exp, scale=SCALE / W_SCALE).then_inc(exp_done, 1)

            def att_split(b, g, first):
                act.wait_ge(att_done, b * G + g + 1)
                if g == 0 and not first:
                    act.wait_ge(o_ready, b * FILLS)
                act.activation(aT[:, 0, g, :], att[:, g % 2], ACT.Copy).then_inc(a_hi, 1)

            def iteration(b, first, last):
                for n in range(STEPS):
                    if not last:
                        if n in K_STEPS:
                            k_split(b + 1, K_STEPS.index(n))
                        if n in Z_STEPS:
                            z_split(b + 1, Z_STEPS.index(n))
                    if first:
                        wo_split(n)
                for g in range(G):
                    if not last and g in Q_SPLITS:
                        q_split(b + 1, Q_SPLITS.index(g))
                    exp_step(b, 2 * g, first)
                    exp_step(b, 2 * g + 1, first)
                    if g >= 3:
                        att_split(b, g - 3, first)
                if not last:
                    q_split(b + 1, 3)
                for g in (G - 3, G - 2, G - 1):
                    att_split(b, g, first)

            for m in range(KT):
                wq_split(m)
            for i in (0, 1):
                k_split(0, i)
            for i in range(FILLS):
                z_split(0, i)
            for i in (2, 3):
                k_split(0, i)
            act.wait_ge(bias_done, KT)
            for i in range(FILLS):
                q_split(0, i)
            iteration(0, True, False)
            with act.Fori(1, B - 1) as b:
                iteration(b, False, False)
            iteration(B - 1, False, True)

        @block.vector
        def _(dve):
            def q_bias_of(m):
                if m:
                    dve.wait_ge(bias_done, m)
                dve.wait_ge(w_in[m % 4], (m // 4 + 1) * DMA)
                dve.scalar_tensor_tensor(out=psum_t[:].rearrange("p j s -> p (j s)"), in0=w_nat[:, m % 4], scalar=W_SCALE,
                                         in1=beta_b[:], op0=ALU.mult, op1=ALU.mult,
                                         accum_out=q_bias[:, m:m + 1]).then_inc(bias_done, 1)

            def wq_split(m):
                dve.wait_ge(wq_hi, m + 1)
                at = slice(m * P, (m + 1) * P)
                dve.scalar_tensor_tensor(out=wqT[:, 1, :, at], in0=score[m % 2][:].rearrange("p j (a o) -> p (j a) o", o=P),
                                         scalar=W_SCALE, in1=wqT[:, 0, :, at], op0=ALU.mult, op1=ALU.subtract).then_inc(wq_lo, 1)

            def wo_split(f):
                m, h = f // 2, f % 2
                dve.wait_ge(wo_hi, f + 1)
                at = slice(m * P, (m + 1) * P)
                dve.scalar_tensor_tensor(out=woT[:, 1, 4 * h:4 * h + 4, at], in0=mm[f % 2][:].rearrange("p (a o) -> p a o", o=P),
                                         scalar=W_SCALE, in1=woT[:, 0, 4 * h:4 * h + 4, at], op0=ALU.mult, op1=ALU.subtract).then_inc(wo_lo, 1)

            def k_split(a, i):
                dve.wait_ge(k_hi, a * FILLS + i + 1)
                dve.tensor_tensor(kT[:, 1, 2 * i:2 * i + 2, :], pv[i % 2][:], kT[:, 0, 2 * i:2 * i + 2, :], ALU.subtract).then_inc(k_lo, 1)

            def z_split(a, i):
                dve.wait_ge(z_hi, a * FILLS + i + 1)
                dve.tensor_tensor(zT[:, 1, 2 * i:2 * i + 2, :], pv[i % 2][:], zT[:, 0, 2 * i:2 * i + 2, :], ALU.subtract).then_inc(z_lo, 1)

            def q_split(a, i):
                dve.wait_ge(q_hi, a * FILLS + i + 1)
                for m2 in range(2):
                    m = 2 * i + m2
                    last = dve.scalar_tensor_tensor(out=qT[:, 1, m, :], in0=mm[i % 2][:, m2 * S:(m2 + 1) * S], scalar=q_bias[:, m:m + 1],
                                                    in1=qT[:, 0, m, :], op0=ALU.add, op1=ALU.subtract)
                last.then_inc(q_lo, 1)

            def row_stats(a, st):
                if st == 0:
                    dve.wait_ge(x_in, (a + 1) * DMA)
                for h in range(2):
                    last = dve.bn_stats(stats[:, st, h, :], x_nat[:, st, h * 512:(h + 1) * 512])
                last.then_inc(bn_done, 1)
                if st == ST - 1:
                    dve.wait_ge(bn_done, (a + 1) * ST)

            def row_rstd(a):
                for st in range(ST):
                    dve.bn_aggr(mean_var[:, st, :], stats[:, st]).then_inc(aggr_done, 1)
                dve.wait_ge(aggr_done, (a + 1) * ST)
                dve.tensor_scalar(var_eps[:], mean_var[:, :, 1], LN_EPS, None, ALU.add).then_inc(rstd_step, 1)
                dve.wait_ge(rstd_step, a * RSTD_STEPS + 1)
                dve.tensor_scalar(newton[:].bitcast(I32), var_eps[:].bitcast(I32), 1, None, ALU.logical_shift_right).then_inc(rstd_step, 1)
                dve.wait_ge(rstd_step, a * RSTD_STEPS + 2)
                dve.tensor_scalar(rstd[:].bitcast(I32), newton[:].bitcast(I32), -1.0, float(0x5F3759DF), ALU.mult, ALU.add).then_inc(rstd_step, 1)
                for k in range(NEWTON):
                    at = a * RSTD_STEPS + 3 + 4 * k
                    dve.wait_ge(rstd_step, at)
                    dve.tensor_tensor(newton[:], rstd[:], rstd[:], ALU.mult).then_inc(rstd_step, 1)
                    dve.wait_ge(rstd_step, at + 1)
                    dve.tensor_tensor(newton[:], newton[:], var_eps[:], ALU.mult).then_inc(rstd_step, 1)
                    dve.wait_ge(rstd_step, at + 2)
                    dve.tensor_scalar(newton[:], newton[:], -0.5, 1.5, ALU.mult, ALU.add).then_inc(rstd_step, 1)
                    dve.wait_ge(rstd_step, at + 3)
                    dve.tensor_tensor(rstd[:], rstd[:], newton[:], ALU.mult).then_inc(rstd_step, 1)

            def normalise(a, st):
                dve.wait_ge(rstd_step, (a + 1) * RSTD_STEPS)
                dve.tensor_scalar(x_nat[:, st], x_nat[:, st], mean_var[:, st, 0:1], rstd[:, st:st + 1],
                                  ALU.subtract, ALU.mult).then_inc(z_done, 1)

            def max_step(b, n):
                g, st = n // 2, n % 2
                dve.wait_ge(s_ready, b * STEPS + n + 1)
                if n == 0 and not (isinstance(b, int) and b == 0):
                    dve.wait_ge(mt_ready, b)
                dve.reduce_max(maxes[:, st, g // HALF, :, g % HALF], score[n % 2][:], AX.X).then_inc(max_done, 1)

            def max_rows(b):
                dve.wait_ge(mt_ready, b + 1)
                if not (isinstance(b, int) and b == 0):
                    dve.wait_ge(m_in, b * DMA)
                dve.tensor_scalar(m_rows[:], pv[0][0:H, 0, :], -1.0 / M_UNIT, None, ALU.mult).then_inc(m_done, 1)

            def divide(b, g, first):
                dve.wait_ge(pv_ready, b * G + g + 1)
                if not (first and g < 1):
                    dve.wait_ge(att_done, b * G + g)
                dve.reciprocal(den[:], pv[g % 2][:, 1, :]).then_inc(den_done, 1)
                dve.wait_ge(den_done, b * G + g + 1)
                if not (first and g < 2):
                    dve.wait_ge(a_lo, b * G + g - 1)
                dve.tensor_tensor(att[:, g % 2], pv[g % 2][:, 0, :], den[:], ALU.mult).then_inc(att_done, 1)

            def att_split(b, g):
                dve.wait_ge(a_hi, b * G + g + 1)
                dve.tensor_tensor(aT[:, 1, g, :], att[:, g % 2], aT[:, 0, g, :], ALU.subtract).then_inc(a_lo, 1)

            def add_residual(c, i):
                dve.wait_ge(o_ready, c * FILLS + i + 1)
                dve.wait_ge(res_in[i % 2], (c * 2 + i // 2 + 1) * DMA)
                if i >= 2:
                    dve.wait_ge(out_done[i % 2], (c * 2 + 1) * DMA)
                elif not (isinstance(c, int) and c == 0):
                    dve.wait_ge(out_done[i % 2], c * 2 * DMA)
                dve.scalar_tensor_tensor(out=o_buf[:, i % 2, :], in0=mm[i % 2][:], scalar=1.0 / W_SCALE, in1=res[:, i % 2, :],
                                         op0=ALU.mult, op1=ALU.add).then_inc(o_done, 1)

            def iteration(b, first, last, more):
                for n in range(STEPS):
                    max_step(b, n)
                    if not last:
                        if n - 1 in K_STEPS:
                            k_split(b + 1, K_STEPS.index(n - 1))
                        if n - 1 in Z_STEPS:
                            z_split(b + 1, Z_STEPS.index(n - 1))
                    if first and n >= 1:
                        wo_split(n - 1)
                    if not first and n in (O_ADDS_LAST if last else O_ADDS):
                        add_residual(b - 1, (O_ADDS_LAST if last else O_ADDS).index(n))
                max_rows(b)
                if first:
                    wo_split(STEPS - 1)
                elif last:
                    add_residual(b - 1, 2)
                else:
                    add_residual(b - 1, 3)
                for g in range(G):
                    if more and g == 0:
                        row_stats(b + 2, 0)
                        row_stats(b + 2, 1)
                    if not last and g in Q_SPLITS:
                        q_split(b + 1, Q_SPLITS.index(g))
                    if g >= 2:
                        divide(b, g - 2, first)
                    if more and g == 1:
                        row_rstd(b + 2)
                    if more and g == 2:
                        normalise(b + 2, 0)
                        normalise(b + 2, 1)
                    if g >= 3:
                        att_split(b, g - 3)
                    if last and g == 1:
                        add_residual(b - 1, 3)
                divide(b, G - 2, first)
                att_split(b, G - 3)
                if not last:
                    q_split(b + 1, 3)
                divide(b, G - 1, first)
                att_split(b, G - 2)
                att_split(b, G - 1)

            O_ADDS, O_ADDS_LAST = (4, 6, 8), (7, 13)
            dve.memset(ones_v[:], 1.0).then_inc(consts, 1)
            dve.memset(rows[0:1, 0, :], 1.0).then_inc(consts, 1)
            dve.memset(rows[0:1, 1, :], M_UNIT).then_inc(consts, 1)
            dve.wait_ge(gb_in, 2 * DMA)
            for m in range(KT):
                q_bias_of(m)
                if m == 2:
                    row_stats(0, 0)
                    row_stats(0, 1)
                if m == 3:
                    row_rstd(0)
                if m == 4:
                    normalise(0, 0)
                    normalise(0, 1)
                if m >= 2:
                    wq_split(m - 2)
            wq_split(KT - 2)
            wq_split(KT - 1)
            for i in (0, 1):
                k_split(0, i)
            for i in range(FILLS):
                z_split(0, i)
            for i in (2, 3):
                k_split(0, i)
            dve.wait_ge(mask_in, DMA)
            dve.tensor_scalar(mask_add[:], mask_u8[:], -1.0, 3e38, ALU.add, ALU.mult).then_inc(mask_ok, 1)
            q_split(0, 0)
            q_split(0, 1)
            row_stats(1, 0)
            row_stats(1, 1)
            row_rstd(1)
            q_split(0, 2)
            for st in range(ST):
                normalise(1, st)
            q_split(0, 3)
            iteration(0, True, False, True)
            with dve.Fori(1, B - 2) as b:
                iteration(b, False, False, True)
            iteration(B - 2, False, False, False)
            iteration(B - 1, False, True, False)
            for i in range(FILLS):
                add_residual(B - 1, i)


_INS = ["x", "ctx_4096", "mask_BxS2_bf1", "L0_xattn_Wq", "L0_xattn_Wout", "L0_xattn_ln_gamma", "L0_xattn_ln_beta"]


def kernel(**inputs):
    import concourse.bacc as bacc
    from concourse.bass_utils import run_bass_kernel_spmd

    nc = bacc.Bacc("TRN2", target_bir_lowering=False, num_devices=1)
    arrays, args = {}, []
    for name in _INS:
        a = np.ascontiguousarray(inputs[name])
        if a.dtype == np.bool_:
            a = a.view(np.uint8)
        arrays[f"in_{name}"] = a
        args.append(nc.dram_tensor(f"in_{name}", a.shape, mybir.dt.from_np(a.dtype), kind="ExternalInput").ap())
    out = nc.dram_tensor("out", (B, S, D), F32, kind="ExternalOutput").ap()
    xattn(nc, *args, out)
    r = run_bass_kernel_spmd(nc, [arrays], core_ids=[0])
    return r.results[0]["out"]
```

```python
from contextlib import ExitStack

import numpy as np

import concourse.bass as bass
from concourse import mybir
from concourse.alu_op_type import AluOpType as ALU

F32 = mybir.dt.float32
F16 = mybir.dt.float16
U8 = mybir.dt.uint8
I32 = mybir.dt.int32
ACT = mybir.ActivationFunctionType
AX = mybir.AxisListType

B, S, D = 8, 256, 1024
H = 32
DH = D // H
P = 128
KT = D // P
ST = S // P
J = P // DH
G = H // J
LN_EPS = 1e-5
SCALE = float(DH) ** -0.5
W_SCALE = 8.0
M_UNIT = 64.0
PASSES = ((0, 0), (0, 1), (1, 0))
FILLS = 4
STEPS = G * ST
DMA = 16
STACK_DMAS = 3 * J + 1
HALF = G // 2
NEWTON = 3
RSTD_STEPS = 3 + 4 * NEWTON


def xattn(nc, x, ctx_in, mask, wq, wout, gamma, beta, out):
    es = ExitStack()
    with es:
        def sb(name, shape, dt):
            return es.enter_context(nc.sbuf_tensor(name, shape, dt))

        def sem(name):
            return es.enter_context(nc.semaphore(name))

        wqT = sb("wqT", [P, 2, KT, D], F16)
        woT = sb("woT", [P, 2, KT, D], F16)
        q_stack = sb("q_stack", [P, 2, J, G // 2, S], F16)
        k_stack = sb("k_stack", [P, 2, J, G // 2, S], F16)
        zT = sb("zT", [P, 2, KT, S], F16)
        qT = sb("qT", [P, 2, G, S], F16)
        kT = sb("kT", [P, 2, G, S], F16)
        aT = sb("aT", [P, 2, G, S], F16)
        probs = sb("probs", [P, 2, ST, J, S], F32)
        psum_t = sb("probs_sum", [P, J, S], F32)
        v_nat = sb("v_nat", [P, ST, D], F32)
        c_nat = sb("c_nat", [P, ST, D], F32)
        x_nat = sb("x_nat", [P, ST, D], F32)
        den = sb("den", [P, S], F32)
        att = sb("att", [P, 2, S], F32)
        res = sb("res", [P, 2, 512], F32)
        o_buf = sb("o_buf", [P, 2, 512], F32)
        gamma_b = sb("gamma_b", [P, D], F32)
        beta_b = sb("beta_b", [P, D], F32)
        ident = sb("ident", [P, P], F32)
        ones_v = sb("ones_v", [P, DH], F32)
        maxes = sb("maxes", [P, ST, 2, J, G // 2], F32)
        m_rows = sb("m_rows", [H, S], F16)
        rows = sb("rows", [1, 2, S], F16)
        mask_u8 = sb("mask_u8", [1, B, S], U8)
        mask_add = sb("mask_add", [1, B, S], F16)
        stats = sb("stats", [P, ST, 2, 6], F32)
        mean_var = sb("mean_var", [P, ST, 2], F32)
        rstd = sb("rstd", [P, ST], F32)
        var_eps = sb("var_eps", [P, ST], F32)
        newton = sb("newton", [P, ST], F32)
        w_nat = probs[:].rearrange("p a t j s -> p (a t) (j s)")

        score = [es.enter_context(nc.psum_tensor(f"score{i}", [P, J, S], F32)) for i in range(2)]
        pv = [es.enter_context(nc.psum_tensor(f"pv{i}", [P, 2, S], F32)) for i in range(2)]
        mm = [es.enter_context(nc.psum_tensor(f"mm{i}", [P, 512], F32)) for i in range(2)]

        gb_in, mask_in = sem("gb_in"), sem("mask_in")
        w_in = [sem(f"w_in{i}") for i in range(4)]
        x_in, c_in, v_in = sem("x_in"), sem("c_in"), sem("v_in")
        res_in = [sem(f"res_in{i}") for i in range(2)]
        out_done = [sem(f"out_done{i}") for i in range(2)]
        row_in, k_in, q_in = sem("row_in"), [sem(f"k_in{i}") for i in range(2)], [sem(f"q_in{i}") for i in range(2)]
        m_in = sem("m_in")
        consts, ident0, ident_ok, stack0 = sem("consts"), sem("ident0"), sem("ident_ok"), sem("stack0")
        mask_ok = sem("mask_ok")
        wq_ready, wq_hi, wq_lo = sem("wq_ready"), sem("wq_hi"), sem("wq_lo")
        wo_ready, wo_hi, wo_lo = sem("wo_ready"), sem("wo_hi"), sem("wo_lo")
        bn_done, aggr_done, rstd_step, norm_done = sem("bn_done"), sem("aggr_done"), sem("rstd_step"), sem("norm_done")
        gamma_done, z_done = sem("gamma_done"), sem("z_done")
        kt_ready, k_hi, k_lo = sem("kt_ready"), sem("k_hi"), sem("k_lo")
        zt_ready, z_hi, z_lo = sem("zt_ready"), sem("z_hi"), sem("z_lo")
        q_ready, q_hi, q_lo = sem("q_ready"), sem("q_hi"), sem("q_lo")
        s_ready, max_done, mt_ready, m_done = sem("s_ready"), sem("max_done"), sem("mt_ready"), sem("m_done")
        t_ready, exp_done, padd_done, pv_ready = sem("t_ready"), sem("exp_done"), sem("padd_done"), sem("pv_ready")
        den_done, att_done, a_hi, a_lo = sem("den_done"), sem("att_done"), sem("a_hi"), sem("a_lo")
        o_ready, o_done = sem("o_ready"), sem("o_done")

        W_FILLS = 2 * KT
        block = es.enter_context(nc.Block())

        K_STEPS, Z_STEPS = (2, 3, 11, 12), (6, 7, 8, 9)

        Q_SPLITS = (1, 4, 6)

        @block.sync
        def _(sp):
            def load_x(a):
                sp.dma_start(x_nat[:], x[a].rearrange("(c p) d -> p c d", p=P)).then_inc(x_in, DMA)

            def load_c(a):
                sp.dma_start(c_nat[:], ctx_in[a].rearrange("(c p) d -> p c d", p=P)).then_inc(c_in, DMA)

            def load_w(n):
                if n >= KT + 4:
                    sp.wait_ge(wo_ready, 2 * (n - KT - 4) + 2)
                elif n >= 4:
                    sp.wait_ge(wq_ready, 2 * (n - 4) + 2)
                w = wq if n < KT else wout
                m = n % KT
                sp.dma_start(w_nat[:, n % 4], w[m * P:(m + 1) * P, :]).then_inc(w_in[n % 4], DMA)

            def fill_k_rows(h, j):
                for r, part in enumerate((0, 0, 1)):
                    sp.dma_start(k_stack[DH * r:DH * (r + 1), h, j],
                                 kT[DH * j:DH * (j + 1), part, h * HALF:(h + 1) * HALF, :]).then_inc(k_in[h], DMA)

            def fill_k_mask(a, h):
                sp.dma_start(k_stack[96:97, h].rearrange("o j g s -> o (j g) s"),
                             mask_add[0:1, a, :].unsqueeze(1).to_broadcast([1, J * HALF, S])).then_inc(k_in[h], DMA)

            def fill_k_stack(a, h, t_count):
                sp.wait_ge(t_ready, t_count)
                for j in range(J):
                    fill_k_rows(h, j)
                fill_k_mask(a, h)

            def fill_q_stack(a, h):
                sp.wait_ge(q_lo, a * FILLS + 2 * h + 2)
                for j in range(J):
                    for r, part in enumerate((0, 1, 0)):
                        sp.dma_start(q_stack[DH * r:DH * (r + 1), h, j],
                                     qT[DH * j:DH * (j + 1), part, h * HALF:(h + 1) * HALF, :]).then_inc(q_in[h], DMA)
                sp.dma_start(q_stack[97:98, h], q_stack[98:99, h]).then_inc(q_in[h], DMA)

            def load_res(c, i):
                if i >= 2:
                    sp.wait_ge(o_done, c * FILLS + i - 1)
                st, nh = i // 2, i % 2
                sp.dma_start(res[:, i % 2, :], x[c, st * P:(st + 1) * P, nh * 512:(nh + 1) * 512]).then_inc(res_in[i % 2], DMA)

            def store_out(c, i):
                sp.wait_ge(o_done, c * FILLS + i + 1)
                st, nh = i // 2, i % 2
                sp.dma_start(out[c, st * P:(st + 1) * P, nh * 512:(nh + 1) * 512], o_buf[:, i % 2, :]).then_inc(out_done[i % 2], DMA)

            def iteration(b, first, last, more):
                if not first:
                    sp.wait_ge(pv_ready, b * G)
                sp.dma_start(v_nat[:], ctx_in[b].rearrange("(c p) d -> p c d", p=P)).then_inc(v_in, DMA)
                if not first:
                    store_out(b - 1, 0)
                    load_res(b - 1, 2)
                    store_out(b - 1, 1)
                    load_res(b - 1, 3)
                if not first and not last:
                    store_out(b - 1, 2)
                sp.wait_ge(m_done, b + 1)
                sp.dma_start(q_stack[97:98].rearrange("o h j g s -> o (h j g) s"), m_rows[:]).then_inc(m_in, DMA)
                if last:
                    store_out(b - 1, 2)
                if not first:
                    store_out(b - 1, 3)
                if more:
                    sp.wait_ge(zt_ready, (b + 2) * FILLS)
                    load_x(b + 2)
                if not last:
                    sp.wait_ge(k_lo, (b + 2) * FILLS)
                if more:
                    load_c(b + 2)
                load_res(b, 0)
                load_res(b, 1)
                if not last:
                    fill_k_stack(b + 1, 0, b * STEPS + STEPS // 2)
                    fill_q_stack(b + 1, 0)
                    fill_k_stack(b + 1, 1, b * STEPS + STEPS)
                    fill_q_stack(b + 1, 1)

            load_x(0)
            load_w(0)
            sp.dma_start(gamma_b[:], gamma.rearrange("(a d) -> a d", a=1).to_broadcast([P, D])).then_inc(gb_in, DMA)
            sp.dma_start(beta_b[:], beta.rearrange("(a d) -> a d", a=1).to_broadcast([P, D])).then_inc(gb_in, DMA)
            load_w(1)
            sp.dma_start(mask_u8[:], mask.rearrange("(o b) s -> o b s", o=1)).then_inc(mask_in, DMA)
            load_w(2)
            load_w(3)
            load_c(0)
            for n in range(4, KT + 4):
                load_w(n)
            sp.wait_ge(k_lo, 2)
            sp.wait_ge(stack0, 2)
            sp.wait_ge(mask_ok, 1)
            for j in range(J):
                fill_k_rows(0, j)
            fill_k_mask(0, 0)
            sp.wait_ge(zt_ready, FILLS)
            load_x(1)
            sp.wait_ge(kt_ready, FILLS)
            load_c(1)
            load_w(KT + 4)
            sp.wait_ge(consts, 3)
            sp.dma_start(q_stack[96:97].rearrange("o h j g s -> o (h j g) s"), rows[0:1, 0, :].unsqueeze(1).to_broadcast([1, H, S])).then_inc(row_in, DMA)
            sp.dma_start(k_stack[97:98].rearrange("o h j g s -> o (h j g) s"), rows[0:1, 1, :].unsqueeze(1).to_broadcast([1, H, S])).then_inc(row_in, DMA)
            load_w(KT + 5)
            sp.wait_ge(k_lo, FILLS)
            for j in range(J):
                fill_k_rows(1, j)
                if j == 0:
                    load_w(KT + 6)
            fill_k_mask(0, 1)
            load_w(KT + 7)
            fill_q_stack(0, 0)
            fill_q_stack(0, 1)
            iteration(0, True, False, True)
            with sp.Fori(1, B - 2) as b:
                iteration(b, False, False, True)
            iteration(B - 2, False, False, False)
            iteration(B - 1, False, True, False)
            store_out(B - 1, 0)
            load_res(B - 1, 2)
            store_out(B - 1, 1)
            load_res(B - 1, 3)
            store_out(B - 1, 2)
            store_out(B - 1, 3)
            for i in range(2):
                sp.wait_ge(out_done[i], B * 2 * DMA)

        @block.gpsimd
        def _(pool):
            pool.memset(ident[:], 0.0).then_inc(ident0, 1)
            pool.wait_ge(ident0, 1)
            pool.affine_select(out=ident[:], in_=ident[:], compare_op=ALU.not_equal, fill=1.0, base=0,
                               pattern=[[-1, P]], channel_multiplier=1).then_inc(ident_ok, 1)

            def scale_and_shift(a):
                for st in range(ST):
                    pool.wait_ge(norm_done, a * ST + st + 1)
                    pool.tensor_tensor(x_nat[:, st], x_nat[:, st], gamma_b[:], ALU.mult).then_inc(gamma_done, 1)
                    pool.wait_ge(gamma_done, a * ST + st + 1)
                    pool.tensor_tensor(x_nat[:, st], x_nat[:, st], beta_b[:], ALU.add).then_inc(z_done, 1)

            pool.wait_ge(gb_in, 2 * DMA)
            scale_and_shift(0)
            pool.wait_ge(z_done, ST)
            for n, stack in enumerate((q_stack, k_stack)):
                if n:
                    pool.wait_ge(stack0, n)
                pool.memset(stack[96:128].rearrange("p h j g s -> p (h j g s)").bitcast(F32), 0.0).then_inc(stack0, 1)
            pool.wait_ge(stack0, 2)

            def iteration(b, first):
                scale_and_shift(b + 1)
                for g in range(G):
                    pool.wait_ge(exp_done, b * STEPS + 2 * g + 2)
                    if not (first and g == 0):
                        pool.wait_ge(pv_ready, b * G + g)
                    pool.tensor_tensor(psum_t[:], probs[:, g % 2, 0], probs[:, g % 2, 1], ALU.add).then_inc(padd_done, 1)

            iteration(0, True)
            with pool.Fori(1, B - 1) as b:
                iteration(b, False)

        @block.tensor
        def _(pe):
            def wq_transposes(f):
                m, h = f // 2, f % 2
                pe.wait_ge(w_in[m % 4], (m // 4 + 1) * DMA)
                if f >= 4:
                    pe.wait_ge(wq_lo, f - 3)
                for n in range(4):
                    k = 4 * h + n
                    last = pe.transpose(score[m % 2][:, 2 * h + n // 2, n % 2 * P:(n % 2 + 1) * P], w_nat[:, m % 4, k * P:(k + 1) * P], ident[:])
                last.then_inc(wq_ready, 1)

            def wo_transposes(f):
                m, h = f // 2, f % 2
                pe.wait_ge(w_in[m % 4], ((KT + m) // 4 + 1) * DMA)
                if f < 2:
                    pe.wait_ge(k_lo, 3 + f)
                else:
                    pe.wait_ge(wo_lo, f - 1)
                for n in range(4):
                    k = 4 * h + n
                    last = pe.transpose(pv[f % 2][:, n // 2, n % 2 * P:(n % 2 + 1) * P], w_nat[:, m % 4, k * P:(k + 1) * P], ident[:])
                last.then_inc(wo_ready, 1)

            def k_transposes(a, i, b):
                if i == 0:
                    pe.wait_ge(c_in, (a + 1) * DMA)
                if i >= 2:
                    pe.wait_ge(z_lo, a * FILLS + i + 1)
                elif isinstance(b, int) and b == 0:
                    pe.wait_ge(wo_lo, W_FILLS - 1 + i)
                elif b is not None:
                    pe.wait_ge(att_done, b * G)
                for n in range(4):
                    g, tt = 2 * i + n // 2, n % 2
                    last = pe.transpose(pv[i % 2][:, n // 2, tt * P:(tt + 1) * P], c_nat[:, tt, g * P:(g + 1) * P], ident[:])
                last.then_inc(kt_ready, 1)

            def z_transposes(a, i):
                if i == 0:
                    pe.wait_ge(z_done, (a + 1) * ST)
                if i < 2:
                    pe.wait_ge(k_lo, a * FILLS + i + 1)
                else:
                    pe.wait_ge(z_lo, a * FILLS + i - 1)
                for n in range(4):
                    k, st = 2 * i + n // 2, n % 2
                    last = pe.transpose(pv[i % 2][:, n // 2, st * P:(st + 1) * P], x_nat[:, st, k * P:(k + 1) * P], ident[:])
                last.then_inc(zt_ready, 1)

            Q_MM = 2 * KT * 3

            def q_matmuls(a, lo, hi, c):
                for u in range(lo, hi):
                    i, v = divmod(u, Q_MM)
                    m2, v2 = divmod(v, KT * 3)
                    k, p = divmod(v2, 3)
                    if u == 0:
                        pe.wait_ge(z_lo, (a + 1) * FILLS)
                    if v == 0 and i >= 2:
                        pe.wait_ge(q_lo, a * FILLS + i - 1)
                    elif v == 0 and c is not None:
                        pe.wait_ge(o_done, c * FILLS + i + 3)
                    elif v == 0 and not (isinstance(a, int) and a == 0):
                        pe.wait_ge(q_lo, (a - 1) * FILLS + i + 3)
                    m = 2 * i + m2
                    wp, zp = PASSES[p]
                    last = pe.matmul(mm[i % 2][:, m2 * S:(m2 + 1) * S], wqT[:, wp, k, m * P:(m + 1) * P], zT[:, zp, k, :],
                                     start=(v2 == 0), stop=(v2 == KT * 3 - 1))
                    if v == Q_MM - 1:
                        last.then_inc(q_ready, 1)

            O_MM = KT * 3
            O_ORDER = [(0, k) for k in range(7)] + [(1, k) for k in range(4)] + [(0, 7)] + [(1, k) for k in range(4, 8)]
            O_ORDER += [(i, k) for i in (2, 3) for k in range(KT)]

            def o_matmuls(c, lo, hi, q_before):
                for u in range(lo, hi):
                    (i, k), p = O_ORDER[u // 3], u % 3
                    v = 3 * k + p
                    st, nh = i // 2, i % 2
                    if u == 0:
                        pe.wait_ge(a_lo, c * G + 5)
                    if u in (3 * O_ORDER.index((0, 5)), 3 * O_ORDER.index((0, 6)), 3 * O_ORDER.index((0, 7))):
                        pe.wait_ge(a_lo, c * G + k + 1)
                    if v == 0 and i >= 2:
                        pe.wait_ge(o_done, c * FILLS + i - 1)
                    elif v == 0 and q_before:
                        pe.wait_ge(q_lo, (c + 1) * FILLS + i + 3)
                    elif v == 0:
                        pe.wait_ge(o_done, (c - 1) * FILLS + i + 3)
                    ap, wp = PASSES[p]
                    last = pe.matmul(mm[i % 2][:], aT[:, ap, k, st * P:(st + 1) * P], woT[:, wp, k, nh * 512:(nh + 1) * 512],
                                     start=(v == 0), stop=(v == O_MM - 1))
                    if v == O_MM - 1:
                        last.then_inc(o_ready, 1)

            def scores_s(b, n, first):
                g, st = n // 2, n % 2
                h, gl = divmod(g, HALF)
                if n in (0, STEPS // 2):
                    pe.wait_ge(k_in[g // HALF], (b + 1) * STACK_DMAS * DMA)
                    pe.wait_ge(q_in[g // HALF], (b + 1) * STACK_DMAS * DMA)
                if n >= 2:
                    pe.wait_ge(max_done, b * STEPS + n - 1)
                elif not first:
                    pe.wait_ge(exp_done, b * STEPS + n - 1)
                else:
                    pe.wait_ge(wq_lo, W_FILLS - 2 + 2 * n)
                for j in range(J):
                    last = pe.matmul(score[n % 2][:, j, :], q_stack[:, h, j, gl, st * P:(st + 1) * P], k_stack[:, h, j, gl, :],
                                     start=True, stop=True)
                last.then_inc(s_ready, 1)

            def max_transposes(b, last_batch):
                pe.wait_ge(max_done, (b + 1) * STEPS)
                if last_batch:
                    pe.wait_ge(att_done, b * G)
                else:
                    pe.wait_ge(k_lo, (b + 1) * FILLS + 3)
                for st in range(ST):
                    last = pe.transpose(pv[0][0:H, 0, st * P:(st + 1) * P], maxes[:, st].rearrange("p h j g -> p (h j g)"), ident[:])
                last.then_inc(mt_ready, 1)

            def scores_t(b, n):
                g, tt = n // 2, n % 2
                h, gl = divmod(g, HALF)
                if n == 0:
                    pe.wait_ge(m_in, (b + 1) * DMA)
                if n < 2:
                    pe.wait_ge(max_done, b * STEPS + STEPS - 1 + n)
                else:
                    pe.wait_ge(exp_done, b * STEPS + n - 1)
                for j in range(J):
                    last = pe.matmul(score[n % 2][:, j, :], k_stack[:, h, j, gl, tt * P:(tt + 1) * P], q_stack[:, h, j, gl, :],
                                     start=True, stop=True)
                last.then_inc(t_ready, 1)

            def probs_times_v(b, g, last_batch):
                pe.wait_ge(exp_done, b * STEPS + 2 * g + 2)
                if g == 0:
                    pe.wait_ge(v_in, (b + 1) * DMA)
                    pe.wait_ge(m_done, b + 1)
                elif g == 1 and not last_batch:
                    pe.wait_ge(k_lo, (b + 2) * FILLS)
                elif g == 1:
                    pe.wait_ge(att_done, b * G)
                else:
                    pe.wait_ge(att_done, b * G + g - 1)
                for tt in range(ST):
                    for j in range(J):
                        pe.matmul(pv[g % 2][DH * j:DH * (j + 1), 0, :], v_nat[:, tt, g * P + DH * j:g * P + DH * (j + 1)],
                                  probs[:, g % 2, tt, j, :], start=(tt == 0), stop=(tt == ST - 1), skip_group_check=True)
                if last_batch:
                    for tt in range(ST):
                        for j in range(J):
                            last = pe.matmul(pv[g % 2][DH * j:DH * (j + 1), 1, :], ones_v[:], probs[:, g % 2, tt, j, :],
                                             start=False, stop=(tt == ST - 1), skip_group_check=True)
                else:
                    pe.wait_ge(padd_done, b * G + g + 1)
                    for j in range(J):
                        last = pe.matmul(pv[g % 2][DH * j:DH * (j + 1), 1, :], ones_v[:], psum_t[:, j, :],
                                         start=False, stop=True, skip_group_check=True)
                last.then_inc(pv_ready, 1)

            O_AT = [6 * n for n in range(STEPS + 1)]
            O_AT_LAST = [4 * n for n in range(STEPS + 1)] + [80, 88] + [4 * O_MM] * (G - 1)
            Q_AT = [40 + 17 * g for g in range(G)] + [172, 4 * Q_MM]
            Q_AT_STEP = [0] * 11 + [8 * n for n in range(STEPS - 10)]
            Q_AT_FIRST = [84 + 12 * g for g in range(G)] + [176, 4 * Q_MM]

            def iteration(b, first, last):
                for n in range(STEPS):
                    scores_s(b, n, first)
                    if not last:
                        if n in K_STEPS:
                            k_transposes(b + 1, K_STEPS.index(n), b)
                        if n in Z_STEPS:
                            z_transposes(b + 1, Z_STEPS.index(n))
                    if not first:
                        at = O_AT_LAST if last else O_AT
                        o_matmuls(b - 1, at[n], at[n + 1], True)
                    else:
                        q_matmuls(b + 1, Q_AT_STEP[n], Q_AT_STEP[n + 1], None)
                max_transposes(b, last)
                q_at = Q_AT_FIRST if first else Q_AT
                if last:
                    o_matmuls(b - 1, O_AT_LAST[STEPS], O_AT_LAST[STEPS + 1], True)
                else:
                    q_matmuls(b + 1, Q_AT_STEP[STEPS] if first else 0, q_at[0], None if first else b - 1)
                for g in range(G):
                    scores_t(b, 2 * g)
                    scores_t(b, 2 * g + 1)
                    if last:
                        o_matmuls(b - 1, O_AT_LAST[STEPS + 1 + g], O_AT_LAST[STEPS + 2 + g], True)
                    else:
                        q_matmuls(b + 1, q_at[g], q_at[g + 1], None if first else b - 1)
                    if g >= 1:
                        probs_times_v(b, g - 1, last)
                if not last:
                    q_matmuls(b + 1, q_at[G], q_at[G + 1], None if first else b - 1)
                else:
                    o_matmuls(b, 0, 5 * 3, False)
                probs_times_v(b, G - 1, last)

            pe.wait_ge(ident_ok, 1)
            for f in range(W_FILLS):
                wq_transposes(f)
            for i in (0, 1):
                k_transposes(0, i, None)
            for i in range(FILLS):
                z_transposes(0, i)
            for i in (2, 3):
                k_transposes(0, i, None)
            pe.wait_ge(wq_lo, W_FILLS)
            for m in range(KT):
                q_matmuls(0, m * Q_MM // 2, (m + 1) * Q_MM // 2, None)
                wo_transposes(2 * m)
                wo_transposes(2 * m + 1)
            pe.wait_ge(row_in, 2 * DMA)
            pe.wait_ge(consts, 3)
            iteration(0, True, False)
            with pe.Fori(1, B - 1) as b:
                iteration(b, False, False)
            iteration(B - 1, False, True)
            o_matmuls(B - 1, 5 * 3, 4 * O_MM, False)

        @block.scalar
        def _(act):
            def wq_split(f):
                m, h = f // 2, f % 2
                act.wait_ge(wq_ready, f + 1)
                act.activation(wqT[:, 0, 4 * h:4 * h + 4, m * P:(m + 1) * P],
                               score[m % 2][:, 2 * h:2 * h + 2].rearrange("p j (a o) -> p (j a) o", o=P), ACT.Copy, scale=W_SCALE).then_inc(wq_hi, 1)

            def wo_split(f):
                m, h = f // 2, f % 2
                act.wait_ge(wo_ready, f + 1)
                act.activation(woT[:, 0, 4 * h:4 * h + 4, m * P:(m + 1) * P], pv[f % 2][:].rearrange("p c (a o) -> p (c a) o", o=P),
                               ACT.Copy, scale=W_SCALE).then_inc(wo_hi, 1)

            def k_split(a, i):
                act.wait_ge(kt_ready, a * FILLS + i + 1)
                if i % 2 == 0 and not (isinstance(a, int) and a == 0):
                    act.wait_ge(k_in[i // 2], a * STACK_DMAS * DMA)
                act.activation(kT[:, 0, 2 * i:2 * i + 2, :], pv[i % 2][:], ACT.Copy).then_inc(k_hi, 1)

            def z_split(a, i):
                act.wait_ge(zt_ready, a * FILLS + i + 1)
                if i == 0 and not (isinstance(a, int) and a == 0):
                    act.wait_ge(q_ready, a * FILLS)
                act.activation(zT[:, 0, 2 * i:2 * i + 2, :], pv[i % 2][:], ACT.Copy).then_inc(z_hi, 1)

            def q_split(a, i):
                act.wait_ge(q_ready, a * FILLS + i + 1)
                if i % 2 == 0 and not (isinstance(a, int) and a == 0):
                    act.wait_ge(q_in[i // 2], a * STACK_DMAS * DMA)
                act.activation(qT[:, 0, 2 * i:2 * i + 2, :].rearrange("p m s -> p (m s)"), mm[i % 2][:], ACT.Copy).then_inc(q_hi, 1)

            def exp_step(b, n, first):
                g, tt = n // 2, n % 2
                act.wait_ge(t_ready, b * STEPS + n + 1)
                if tt == 0 and not (first and g < 2):
                    act.wait_ge(pv_ready, b * G + g - 1)
                act.activation(probs[:, g % 2, tt], score[n % 2][:], ACT.Exp, scale=SCALE / W_SCALE).then_inc(exp_done, 1)

            def att_split(b, g, first):
                act.wait_ge(att_done, b * G + g + 1)
                if g == 0 and not first:
                    act.wait_ge(o_ready, b * FILLS)
                act.activation(aT[:, 0, g, :], att[:, g % 2], ACT.Copy).then_inc(a_hi, 1)

            def iteration(b, first, last):
                for n in range(STEPS):
                    if not last:
                        if n in K_STEPS:
                            k_split(b + 1, K_STEPS.index(n))
                        if n in Z_STEPS:
                            z_split(b + 1, Z_STEPS.index(n))
                for g in range(G):
                    if not last and g in Q_SPLITS:
                        q_split(b + 1, Q_SPLITS.index(g))
                    exp_step(b, 2 * g, first)
                    exp_step(b, 2 * g + 1, first)
                    if g >= 3:
                        att_split(b, g - 3, first)
                att_split(b, G - 3, first)
                att_split(b, G - 2, first)
                if not last:
                    q_split(b + 1, 3)
                att_split(b, G - 1, first)

            for f in range(W_FILLS):
                wq_split(f)
            for i in (0, 1):
                k_split(0, i)
            for i in range(FILLS):
                z_split(0, i)
            for i in (2, 3):
                k_split(0, i)
            for m in range(KT):
                if m % 2:
                    q_split(0, m // 2)
                wo_split(2 * m)
                wo_split(2 * m + 1)
            iteration(0, True, False)
            with act.Fori(1, B - 1) as b:
                iteration(b, False, False)
            iteration(B - 1, False, True)

        @block.vector
        def _(dve):
            def wq_split(f):
                m, h = f // 2, f % 2
                dve.wait_ge(wq_hi, f + 1)
                at = slice(m * P, (m + 1) * P)
                dve.scalar_tensor_tensor(out=wqT[:, 1, 4 * h:4 * h + 4, at],
                                         in0=score[m % 2][:, 2 * h:2 * h + 2].rearrange("p j (a o) -> p (j a) o", o=P),
                                         scalar=W_SCALE, in1=wqT[:, 0, 4 * h:4 * h + 4, at], op0=ALU.mult, op1=ALU.subtract).then_inc(wq_lo, 1)

            def wo_split(f):
                m, h = f // 2, f % 2
                dve.wait_ge(wo_hi, f + 1)
                at = slice(m * P, (m + 1) * P)
                dve.scalar_tensor_tensor(out=woT[:, 1, 4 * h:4 * h + 4, at], in0=pv[f % 2][:].rearrange("p c (a o) -> p (c a) o", o=P),
                                         scalar=W_SCALE, in1=woT[:, 0, 4 * h:4 * h + 4, at], op0=ALU.mult, op1=ALU.subtract).then_inc(wo_lo, 1)

            def k_split(a, i):
                dve.wait_ge(k_hi, a * FILLS + i + 1)
                dve.tensor_tensor(kT[:, 1, 2 * i:2 * i + 2, :], pv[i % 2][:], kT[:, 0, 2 * i:2 * i + 2, :], ALU.subtract).then_inc(k_lo, 1)

            def z_split(a, i):
                dve.wait_ge(z_hi, a * FILLS + i + 1)
                dve.tensor_tensor(zT[:, 1, 2 * i:2 * i + 2, :], pv[i % 2][:], zT[:, 0, 2 * i:2 * i + 2, :], ALU.subtract).then_inc(z_lo, 1)

            def q_split(a, i):
                dve.wait_ge(q_hi, a * FILLS + i + 1)
                at = slice(2 * i, 2 * i + 2)
                dve.tensor_tensor(qT[:, 1, at].rearrange("p m s -> p (m s)"), mm[i % 2][:],
                                  qT[:, 0, at].rearrange("p m s -> p (m s)"), ALU.subtract).then_inc(q_lo, 1)

            def row_stats(a, st):
                if st == 0:
                    dve.wait_ge(x_in, (a + 1) * DMA)
                for h in range(2):
                    last = dve.bn_stats(stats[:, st, h, :], x_nat[:, st, h * 512:(h + 1) * 512])
                last.then_inc(bn_done, 1)
                if st == ST - 1:
                    dve.wait_ge(bn_done, (a + 1) * ST)

            def row_rstd(a):
                for st in range(ST):
                    dve.bn_aggr(mean_var[:, st, :], stats[:, st]).then_inc(aggr_done, 1)
                dve.wait_ge(aggr_done, (a + 1) * ST)
                dve.tensor_scalar(var_eps[:], mean_var[:, :, 1], LN_EPS, None, ALU.add).then_inc(rstd_step, 1)
                dve.wait_ge(rstd_step, a * RSTD_STEPS + 1)
                dve.tensor_scalar(newton[:].bitcast(I32), var_eps[:].bitcast(I32), 1, None, ALU.logical_shift_right).then_inc(rstd_step, 1)
                dve.wait_ge(rstd_step, a * RSTD_STEPS + 2)
                dve.tensor_scalar(rstd[:].bitcast(I32), newton[:].bitcast(I32), -1.0, float(0x5F3759DF), ALU.mult, ALU.add).then_inc(rstd_step, 1)
                for k in range(NEWTON):
                    at = a * RSTD_STEPS + 3 + 4 * k
                    dve.wait_ge(rstd_step, at)
                    dve.tensor_tensor(newton[:], rstd[:], rstd[:], ALU.mult).then_inc(rstd_step, 1)
                    dve.wait_ge(rstd_step, at + 1)
                    dve.tensor_tensor(newton[:], newton[:], var_eps[:], ALU.mult).then_inc(rstd_step, 1)
                    dve.wait_ge(rstd_step, at + 2)
                    dve.tensor_scalar(newton[:], newton[:], -0.5, 1.5, ALU.mult, ALU.add).then_inc(rstd_step, 1)
                    dve.wait_ge(rstd_step, at + 3)
                    dve.tensor_tensor(rstd[:], rstd[:], newton[:], ALU.mult).then_inc(rstd_step, 1)

            def normalise(a, st):
                dve.wait_ge(rstd_step, (a + 1) * RSTD_STEPS)
                dve.tensor_scalar(x_nat[:, st], x_nat[:, st], mean_var[:, st, 0:1], rstd[:, st:st + 1],
                                  ALU.subtract, ALU.mult).then_inc(norm_done, 1)

            def max_step(b, n):
                g, st = n // 2, n % 2
                dve.wait_ge(s_ready, b * STEPS + n + 1)
                if n == 0 and not (isinstance(b, int) and b == 0):
                    dve.wait_ge(mt_ready, b)
                dve.reduce_max(maxes[:, st, g // HALF, :, g % HALF], score[n % 2][:], AX.X).then_inc(max_done, 1)

            def max_rows(b):
                dve.wait_ge(mt_ready, b + 1)
                if not (isinstance(b, int) and b == 0):
                    dve.wait_ge(m_in, b * DMA)
                dve.tensor_scalar(m_rows[:], pv[0][0:H, 0, :], -1.0 / M_UNIT, None, ALU.mult).then_inc(m_done, 1)

            def divide(b, g, first):
                dve.wait_ge(pv_ready, b * G + g + 1)
                if not (first and g < 1):
                    dve.wait_ge(att_done, b * G + g)
                dve.reciprocal(den[:], pv[g % 2][:, 1, :]).then_inc(den_done, 1)
                dve.wait_ge(den_done, b * G + g + 1)
                if not (first and g < 2):
                    dve.wait_ge(a_lo, b * G + g - 1)
                dve.tensor_tensor(att[:, g % 2], pv[g % 2][:, 0, :], den[:], ALU.mult).then_inc(att_done, 1)

            def att_split(b, g):
                dve.wait_ge(a_hi, b * G + g + 1)
                dve.tensor_tensor(aT[:, 1, g, :], att[:, g % 2], aT[:, 0, g, :], ALU.subtract).then_inc(a_lo, 1)

            def add_residual(c, i):
                dve.wait_ge(o_ready, c * FILLS + i + 1)
                dve.wait_ge(res_in[i % 2], (c * 2 + i // 2 + 1) * DMA)
                if i >= 2:
                    dve.wait_ge(out_done[i % 2], (c * 2 + 1) * DMA)
                dve.scalar_tensor_tensor(out=o_buf[:, i % 2, :], in0=mm[i % 2][:], scalar=1.0 / W_SCALE, in1=res[:, i % 2, :],
                                         op0=ALU.mult, op1=ALU.add).then_inc(o_done, 1)

            def iteration(b, first, last, more):
                for n in range(STEPS):
                    max_step(b, n)
                    if n == 0 and not first:
                        att_split(b - 1, G - 1)
                    if not last:
                        if n - 1 in K_STEPS:
                            k_split(b + 1, K_STEPS.index(n - 1))
                        if n - 1 in Z_STEPS:
                            z_split(b + 1, Z_STEPS.index(n - 1))
                    if not first and n in (O_ADDS_LAST if last else O_ADDS):
                        add_residual(b - 1, (O_ADDS_LAST if last else O_ADDS).index(n))
                max_rows(b)
                if last:
                    add_residual(b - 1, 2)
                elif not first:
                    add_residual(b - 1, 3)
                for g in range(G):
                    if more and g == 0:
                        row_stats(b + 2, 0)
                        row_stats(b + 2, 1)
                    if not last and g in Q_SPLITS:
                        q_split(b + 1, Q_SPLITS.index(g))
                    if g >= 2:
                        divide(b, g - 2, first)
                    if more and g == 1:
                        row_rstd(b + 2)
                    if more and g == 2:
                        normalise(b + 2, 0)
                        normalise(b + 2, 1)
                    if g >= 3:
                        att_split(b, g - 3)
                    if last and g == 1:
                        add_residual(b - 1, 3)
                divide(b, G - 2, first)
                if not first:
                    for i in range(2):
                        dve.wait_ge(out_done[i], b * 2 * DMA)
                att_split(b, G - 3)
                att_split(b, G - 2)
                if not last:
                    q_split(b + 1, 3)
                divide(b, G - 1, first)
                if last:
                    att_split(b, G - 1)

            O_ADDS, O_ADDS_LAST = (6, 8, 12), (9, 12)
            dve.memset(ones_v[:], 1.0).then_inc(consts, 1)
            dve.memset(rows[0:1, 0, :], 1.0).then_inc(consts, 1)
            dve.memset(rows[0:1, 1, :], M_UNIT).then_inc(consts, 1)
            row_stats(0, 0)
            row_stats(0, 1)
            row_rstd(0)
            for st in range(ST):
                normalise(0, st)
            for f in range(W_FILLS):
                wq_split(f)
                if f == 3:
                    dve.wait_ge(mask_in, DMA)
                    dve.tensor_scalar(mask_add[:], mask_u8[:], -1.0, 3e38, ALU.add, ALU.mult).then_inc(mask_ok, 1)
            for i in (0, 1):
                k_split(0, i)
            for i in range(FILLS):
                z_split(0, i)
            for i in (2, 3):
                k_split(0, i)
            for m in range(KT):
                if m % 2:
                    q_split(0, m // 2)
                wo_split(2 * m)
                wo_split(2 * m + 1)
                if m == 1:
                    row_stats(1, 0)
                    row_stats(1, 1)
                if m == 2:
                    row_rstd(1)
                if m == 3:
                    for st in range(ST):
                        normalise(1, st)
            iteration(0, True, False, True)
            with dve.Fori(1, B - 2) as b:
                iteration(b, False, False, True)
            iteration(B - 2, False, False, False)
            iteration(B - 1, False, True, False)
            for i in range(FILLS):
                add_residual(B - 1, i)


_INS = ["x", "ctx_4096", "mask_BxS2_bf1", "L0_xattn_Wq", "L0_xattn_Wout", "L0_xattn_ln_gamma", "L0_xattn_ln_beta"]


def kernel(**inputs):
    import concourse.bacc as bacc
    from concourse.bass_utils import run_bass_kernel_spmd

    nc = bacc.Bacc("TRN2", target_bir_lowering=False, num_devices=1)
    arrays, args = {}, []
    for name in _INS:
        a = np.ascontiguousarray(inputs[name])
        if a.dtype == np.bool_:
            a = a.view(np.uint8)
        arrays[f"in_{name}"] = a
        args.append(nc.dram_tensor(f"in_{name}", a.shape, mybir.dt.from_np(a.dtype), kind="ExternalInput").ap())
    out = nc.dram_tensor("out", (B, S, D), F32, kind="ExternalOutput").ap()
    xattn(nc, *args, out)
    r = run_bass_kernel_spmd(nc, [arrays], core_ids=[0])
    return r.results[0]["out"]
```
